# Optimizing a Trainium2 kernel written in Bass

```python
import numpy as np
import jax
import jax.numpy as jnp

def _softmax(x, axis=-1):
    return jax.nn.softmax(x, axis=axis)

def _gelu(x):
    return jax.nn.gelu(x, approximate=True)

def _silu(x):
    return jax.nn.silu(x)

def _sigmoid(x):
    return jax.nn.sigmoid(x)

def _layernorm(x, axis=-1, eps=1e-05):
    m = jnp.mean(x, axis=axis, keepdims=True)
    v = jnp.var(x, axis=axis, keepdims=True)
    return (x - m) / jnp.sqrt(v + eps)

def _scatter_add(tgt, idx, src, axis=0):
    return tgt.at[idx].add(src)

def _segment_sum(src, seg, n):
    return jax.ops.segment_sum(src, seg, n)
kernel_name = 'mk_gnn_resnorm_d1_gnn_r32_845110'

def setup_inputs(seed: int=0):
    np.random.seed(seed)
    _w = jnp.asarray

    def _rec_inputs():
        import jax
        import jax.numpy as jnp
        _gk = jax.random.key(seed)
        x = -8.776e-05 + 1 * jax.random.normal(jax.random.fold_in(_gk, 1), (1250, 128), jnp.float32)
        src = jax.random.randint(jax.random.fold_in(_gk, 2), (20000,), 0, 1250, jnp.int32)
        dst = jax.random.randint(jax.random.fold_in(_gk, 3), (20000,), 0, 1250, jnp.int32)
        _o = jnp.argsort(dst, stable=True)
        src = src[_o]
        dst = dst[_o]
        edge_attr_50 = 0.000229061 + 1.00009 * jax.random.normal(jax.random.fold_in(_gk, 11), (20000, 50), jnp.float32)
        edge_weight = jax.random.uniform(jax.random.fold_in(_gk, 13), (20000,), jnp.float32, 0.0, 12)
        return (x, src, dst, edge_attr_50, edge_weight)
    x, src, dst, edge_attr_50, edge_weight = _rec_inputs()

    def _L0_gnn_setup():
        import jax, jax.numpy as jnp
        import numpy as np
        from math import pi as PI
        N, E, H, F, G = (1250, 18750, 128, 128, 50)
        CUTOFF = 10.0
        SQRT_2_OVER_PI = 0.7978845608028654

        def gelu_gt2(x):
            return 0.5 * x * (1.0 + jnp.tanh(SQRT_2_OVER_PI * (x + 0.044715 * x * x * x)))

        def _xavier(key, shape):
            fan_in, fan_out = (shape[0], shape[1])
            lim = jnp.sqrt(6.0 / (fan_in + fan_out)).astype(jnp.float32)
            return jax.random.uniform(key, shape, jnp.float32, -lim, lim)
        key = jax.random.key(seed)
        ks = jax.random.split(key, 12)
        x = jax.random.normal(ks[0], (N, H), jnp.float32)
        edge_index = jax.random.randint(ks[1], (2, E), 0, N, jnp.int32)
        edge_length = jax.random.uniform(ks[2], (E,), jnp.float32) * (CUTOFF * 1.2)
        edge_attr = jax.random.normal(ks[3], (E, G), jnp.float32)
        f_w0 = _xavier(ks[4], (G, F))
        f_b0 = jnp.zeros((F,), jnp.float32)
        f_w1 = _xavier(ks[5], (F, F))
        f_b1 = jnp.zeros((F,), jnp.float32)
        f_w2 = _xavier(ks[6], (F, F))
        f_b2 = jnp.zeros((F,), jnp.float32)
        f_w3 = _xavier(ks[7], (F, F))
        f_b3 = jnp.zeros((F,), jnp.float32)
        lin1_w = _xavier(ks[8], (H, F))
        lin2_w = _xavier(ks[9], (F, H))
        lin2_b = jnp.zeros((H,), jnp.float32)
        lin_w = _xavier(ks[10], (H, H))
        lin_b = jnp.zeros((H,), jnp.float32)
        return dict(x=x, edge_index=edge_index, edge_length=edge_length, edge_attr=edge_attr, f_w0=f_w0, f_b0=f_b0, f_w1=f_w1, f_b1=f_b1, f_w2=f_w2, f_b2=f_b2, f_w3=f_w3, f_b3=f_b3, lin1_w=lin1_w, lin2_w=lin2_w, lin2_b=lin2_b, lin_w=lin_w, lin_b=lin_b)
    _L0_gnn_all = _L0_gnn_setup()
    _L0_gnn_in = {k: v for k, v in _L0_gnn_all.items() if k in ('f_w0', 'f_b0', 'f_w1', 'f_b1', 'f_w2', 'f_b2', 'f_w3', 'f_b3', 'lin1_w', 'lin2_w', 'lin2_b', 'lin_w', 'lin_b')}
    del _L0_gnn_all
    return {'x': x, 'src': src, 'dst': dst, 'edge_attr_50': edge_attr_50, 'edge_weight': edge_weight, 'L0_gnn_f_w0': _L0_gnn_in['f_w0'], 'L0_gnn_f_b0': _L0_gnn_in['f_b0'], 'L0_gnn_f_w1': _L0_gnn_in['f_w1'], 'L0_gnn_f_b1': _L0_gnn_in['f_b1'], 'L0_gnn_f_w2': _L0_gnn_in['f_w2'], 'L0_gnn_f_b2': _L0_gnn_in['f_b2'], 'L0_gnn_f_w3': _L0_gnn_in['f_w3'], 'L0_gnn_f_b3': _L0_gnn_in['f_b3'], 'L0_gnn_lin1_w': _L0_gnn_in['lin1_w'], 'L0_gnn_lin2_w': _L0_gnn_in['lin2_w'], 'L0_gnn_lin2_b': _L0_gnn_in['lin2_b'], 'L0_gnn_lin_w': _L0_gnn_in['lin_w'], 'L0_gnn_lin_b': _L0_gnn_in['lin_b']}

def reference(x, src, dst, edge_attr_50, edge_weight, L0_gnn_f_w0, L0_gnn_f_b0, L0_gnn_f_w1, L0_gnn_f_b1, L0_gnn_f_w2, L0_gnn_f_b2, L0_gnn_f_w3, L0_gnn_f_b3, L0_gnn_lin1_w, L0_gnn_lin2_w, L0_gnn_lin2_b, L0_gnn_lin_w, L0_gnn_lin_b):
    import jax
    import jax.numpy as jnp

    def _L0_gnn_ref(x, edge_index, edge_length, edge_attr, f_w0, f_b0, f_w1, f_b1, f_w2, f_b2, f_w3, f_b3, lin1_w, lin2_w, lin2_b, lin_w, lin_b):
        import jax, jax.numpy as jnp
        import numpy as np
        from math import pi as PI
        N, E, H, F, G = (1250, 18750, 128, 128, 50)
        CUTOFF = 10.0
        SQRT_2_OVER_PI = 0.7978845608028654

        def gelu_gt2(x):
            return 0.5 * x * (1.0 + jnp.tanh(SQRT_2_OVER_PI * (x + 0.044715 * x * x * x)))

        def _xavier(key, shape):
            fan_in, fan_out = (shape[0], shape[1])
            lim = jnp.sqrt(6.0 / (fan_in + fan_out)).astype(jnp.float32)
            return jax.random.uniform(key, shape, jnp.float32, -lim, lim)
        C = 0.5 * (jnp.cos(edge_length * (PI / CUTOFF)) + 1.0)
        C = C * ((edge_length <= CUTOFF) & (edge_length >= 0.0)).astype(x.dtype)
        h = gelu_gt2(edge_attr @ f_w0 + f_b0)
        h = gelu_gt2(h @ f_w1 + f_b1)
        h = gelu_gt2(h @ f_w2 + f_b2)
        h = gelu_gt2(h @ f_w3 + f_b3)
        W = h * C[:, None]
        xf = x @ lin1_w
        src, dst = (edge_index[0], edge_index[1])
        msg = xf[src] * W
        agg = jax.ops.segment_sum(msg, dst, num_segments=N)
        out = agg @ lin2_w + lin2_b
        out = gelu_gt2(out) @ lin_w + lin_b
        return out
    edge_index = jnp.stack([src, dst])
    x = _layernorm(x + _L0_gnn_ref(x, edge_index, edge_weight, edge_attr_50, L0_gnn_f_w0, L0_gnn_f_b0, L0_gnn_f_w1, L0_gnn_f_b1, L0_gnn_f_w2, L0_gnn_f_b2, L0_gnn_f_w3, L0_gnn_f_b3, L0_gnn_lin1_w, L0_gnn_lin2_w, L0_gnn_lin2_b, L0_gnn_lin_w, L0_gnn_lin_b), axis=-1)
    return x

_drawn_inputs = setup_inputs


def setup_inputs(seed=0):
    import zlib

    import numpy as np

    out = dict(_drawn_inputs(seed))
    spreads = {'L0_gnn_f_b0': (0.0, 0.58),
     'L0_gnn_f_b1': (0.0, 0.428),
     'L0_gnn_f_b2': (0.0, 0.315),
     'L0_gnn_f_b3': (0.0, 0.1),
     'L0_gnn_lin2_b': (0.0, 0.1),
     'L0_gnn_lin_b': (0.0, 0.1)}
    factors = {}
    for name, (base, spread) in spreads.items():
        noise = np.random.default_rng([zlib.crc32(name.encode()), seed]).standard_normal(out[name].shape)
        drawn = base * np.exp(spread * noise) if base else spread * noise
        out[name] = jnp.asarray(drawn.astype(out[name].dtype))
    for name, factor in factors.items():
        out[name] = (out[name] * factor).astype(out[name].dtype)
    return out
```

```python
from contextlib import ExitStack

import concourse.bass as bass
from concourse import mybir

NODES, EDGES, FEAT, EDGE_FEAT = 1250, 20000, 128, 50
CUTOFF = 10.0
PI = 3.141592653589793
LN_EPS = 1e-5

TILE = 125
TILES_PER_GROUP = 4
GROUP = TILE * TILES_PER_GROUP
GROUPS = EDGES // GROUP
PAIRS = GROUPS // 2
PAIRS_PER_TURN = 2
GROUPS_PER_TURN = 2 * PAIRS_PER_TURN
TURNS = PAIRS // PAIRS_PER_TURN
NODE_CHUNKS = NODES // TILE

WINDOW = 64
MAX_PASSES = -(-NODES // WINDOW)
AGG_COLS = NODES + WINDOW
ODD_BASE = 64


def gnn_layer(nc, xT, x_nodes, srcT, dstT, dst_groups, weightT, edge_attrT,
              f_w0, f_b0, f_w1, f_b1, f_w2, f_b2, f_w3, f_b3, lin1_w, lin2_w, lin2_b, lin_w, lin_b, out):
    fp32 = mybir.dt.float32
    int32 = mybir.dt.int32
    ALU = mybir.AluOpType
    ACT = mybir.ActivationFunctionType
    AX_X = mybir.AxisListType.X
    GELU = ACT.Gelu_apprx_tanh

    with ExitStack() as ctx:
        def sb(name, shape, dt=fp32):
            return ctx.enter_context(nc.sbuf_tensor(name, shape, dt))

        def sem(name):
            return ctx.enter_context(nc.semaphore(name))

        xT_sb = sb("xT_sb", [FEAT, NODES])
        x_sb = sb("x_sb", [TILE, NODE_CHUNKS, FEAT])
        lin1_sb = sb("lin1_sb", [FEAT, FEAT])
        w0_sb = sb("w0_sb", [ODD_BASE + EDGE_FEAT, FEAT])
        w1_sb = sb("w1_sb", [FEAT, FEAT])
        w2_sb = sb("w2_sb", [FEAT, FEAT])
        w3_sb = sb("w3_sb", [FEAT, FEAT])
        lin2_sb = sb("lin2_sb", [FEAT, FEAT])
        lin_sb = sb("lin_sb", [FEAT, FEAT])
        b0_sb = sb("b0_sb", [FEAT, 1])
        b1_sb = sb("b1_sb", [FEAT, 1])
        b2_sb = sb("b2_sb", [FEAT, 1])
        lin2_b_sb = sb("lin2_b_sb", [FEAT, 1])
        b3_sb = sb("b3_sb", [TILE, FEAT])
        lin_b_sb = sb("lin_b_sb", [TILE, FEAT])
        xf_sb = sb("xf_sb", [TILE, NODE_CHUNKS, FEAT])
        xf_dram = nc.dram_tensor("xf_dram", [NODES, FEAT], fp32, kind="Internal").ap()

        dst_i = sb("dst_i", [TILE, GROUPS, TILES_PER_GROUP], int32)
        dst_f = sb("dst_f", [TILE, GROUPS, TILES_PER_GROUP])
        dst_rel = sb("dst_rel", [TILE, GROUPS, TILES_PER_GROUP])
        dist = sb("dist", [TILE, GROUPS * TILES_PER_GROUP])
        clamped = sb("clamped", [TILE, GROUPS * TILES_PER_GROUP])
        cosine = sb("cosine", [TILE, GROUPS * TILES_PER_GROUP])
        inside = sb("inside", [TILE, GROUPS * TILES_PER_GROUP])
        not_above = sb("not_above", [TILE, GROUPS * TILES_PER_GROUP])
        half_cos = sb("half_cos", [TILE, GROUPS * TILES_PER_GROUP])
        cut = sb("cut", [TILE, GROUPS, TILES_PER_GROUP])
        half_pi = sb("half_pi", [TILE, 1])

        dstg_i = sb("dstg_i", [GROUPS, GROUP], int32)
        dstg_f = sb("dstg_f", [GROUPS, GROUP])
        lo_hi = sb("lo_hi", [GROUPS, 2])
        span = sb("span", [GROUPS, 1])
        ident = sb("ident", [GROUPS, GROUPS])
        ones = sb("ones", [GROUPS, TILE])
        diag = sb("diag", [GROUPS, 2, GROUPS])
        iota_i = sb("iota_i", [TILE, MAX_PASSES * WINDOW], int32)
        iota_f = sb("iota_f", [TILE, MAX_PASSES * WINDOW])
        max_span = sb("max_span", [1, 1])
        pass_needed = sb("pass_needed", [1, MAX_PASSES])
        passes_f = sb("passes_f", [1, 1])
        passes_i = sb("passes_i", [1, 1], int32)
        base_raw = sb("base_raw", [1, MAX_PASSES, GROUPS])
        base_col = sb("base_col", [1, 2 + MAX_PASSES * GROUPS], int32)

        edge_in = sb("edge_in", [ODD_BASE + EDGE_FEAT, PAIRS_PER_TURN, GROUP])
        src_idx = sb("src_idx", [TILE, PAIRS_PER_TURN, 2 * TILES_PER_GROUP], int32)
        gathered = sb("gathered", [TILE, GROUPS_PER_TURN, TILES_PER_GROUP, FEAT])
        h1 = sb("h1", [FEAT, 2, GROUP])
        h2 = sb("h2", [FEAT, 2, GROUP])
        h3 = sb("h3", [FEAT, 2, GROUP])
        pre4 = sb("pre4", [TILE, 2, TILES_PER_GROUP, FEAT])
        h4 = sb("h4", [TILE, 2, TILES_PER_GROUP, FEAT])
        message = sb("message", [TILE, GROUPS_PER_TURN, TILES_PER_GROUP, FEAT])
        hit = sb("hit", [TILE, GROUPS_PER_TURN, TILES_PER_GROUP, WINDOW])
        onehot = sb("onehot", [TILE, GROUPS_PER_TURN, TILES_PER_GROUP, WINDOW])
        aggT = sb("aggT", [FEAT, AGG_COLS])

        nodeT = sb("nodeT", [FEAT, NODES])
        resid = sb("resid", [TILE, NODE_CHUNKS, FEAT])
        x_plus_b = sb("x_plus_b", [TILE, NODE_CHUNKS, FEAT])
        stats = sb("stats", [TILE, NODE_CHUNKS, 6])
        mean_var = sb("mean_var", [TILE, NODE_CHUNKS, 2])
        std = sb("std", [TILE, NODE_CHUNKS])
        eps = sb("eps", [TILE, 1])
        rstd = sb("rstd", [TILE, NODE_CHUNKS])
        normed = sb("normed", [TILE, NODE_CHUNKS, FEAT])

        def bank(name):
            return ctx.enter_context(nc.psum_tensor(name, [128, 512], fp32))

        ps1 = [bank("ps1_even"), bank("ps1_odd")]
        ps23 = [bank("ps23_even"), bank("ps23_odd")]
        ps4 = [bank("ps4_even"), bank("ps4_odd")]
        ps_agg = [bank("ps_agg_even"), bank("ps_agg_odd")]

        chunk_cuts = ((0, 4), (4, 8), (8, NODE_CHUNKS))
        node_cuts = [(c0 * TILE, c1 * TILE) for c0, c1 in chunk_cuts]
        xf_bank = (ps4[0], ps4[1], ps_agg[1])
        node_bank = (ps1[0], ps1[1], ps23[0])
        out_bank = (ps4[0], ps4[1], ps23[1])

        x_loaded = sem("x_loaded")
        tables_loaded = sem("tables_loaded")
        w_loaded = sem("w_loaded")
        late_loaded = sem("late_loaded")
        edge_loaded = [sem("edge_loaded_even"), sem("edge_loaded_odd")]
        src_loaded = [sem("src_loaded_even"), sem("src_loaded_odd")]
        xf_product = sem("xf_product")
        xf_copied = sem("xf_copied")
        xf_stored = sem("xf_stored")
        out_stored = sem("out_stored")
        consts_ready = sem("consts_ready")
        diag_ready = sem("diag_ready")
        rows_ready = sem("rows_ready")
        clamped_ready = sem("clamped_ready")
        cosine_ready = sem("cosine_ready")
        setup_step = sem("setup_step")
        plan_ready = sem("plan_ready")
        l1_done = sem("l1_done")
        l2_done = sem("l2_done")
        l3_done = sem("l3_done")
        l4_done = sem("l4_done")
        act1_done = sem("act1_done")
        act2_done = sem("act2_done")
        act3_done = sem("act3_done")
        act4_done = sem("act4_done")
        bias4_done = sem("bias4_done")
        hit_done = sem("hit_done")
        message_done = sem("message_done")
        scatter_done = sem("scatter_done")
        agg_added = sem("agg_added")
        gather_landed = [sem(f"gather_landed_{b}") for b in range(GROUPS_PER_TURN)]
        group_begun = sem("group_begun")
        node2_done = sem("node2_done")
        node_gelu_done = sem("node_gelu_done")
        node3_done = sem("node3_done")
        ln_step = sem("ln_step")
        var_done = sem("var_done")
        std_done = sem("std_done")
        normed_done = sem("normed_done")

        block = ctx.enter_context(nc.Block())

        def flat(r, turn):
            return r * TURNS + turn

        @block.sync
        def _(sp):
            sp.dma_start(xT_sb[:, :], xT).then_inc(x_loaded, 16)
            sp.dma_start(lin1_sb[:, :], lin1_w).then_inc(x_loaded, 16)
            sp.dma_start(dist[:, :], weightT).then_inc(tables_loaded, 16)
            sp.dma_start(dstg_i[:, :], dst_groups).then_inc(tables_loaded, 16)
            sp.dma_start(dst_i[:, :, :].rearrange("p g t -> p (g t)"), dstT).then_inc(tables_loaded, 16)

            def load_edges(pair, q):
                for b in range(2):
                    sp.dma_start(edge_in[b * ODD_BASE:b * ODD_BASE + EDGE_FEAT, q, :],
                                 edge_attrT[bass.ds(pair, 1), b, :, :].rearrange("o f e -> (o f) e"))\
                        .then_inc(edge_loaded[q], 16)

            def load_src(pair, q):
                sp.dma_start(src_idx[:, q, :], srcT[bass.ds(pair, 1), :, :].rearrange("o p t -> (o p) t"))\
                    .then_inc(src_loaded[q], 16)

            load_edges(0, 0)
            for q in range(PAIRS_PER_TURN):
                load_src(q, q)
            sp.wait_ge(xf_copied, 3)
            sp.dma_start(xf_dram.rearrange("(c p) f -> p c f", p=TILE), xf_sb[:, :, :]).then_inc(xf_stored, 16)
            sp.dma_start(x_sb[:, :, :], x_nodes.rearrange("(c p) f -> p c f", p=TILE)).then_inc(late_loaded, 16)
            sp.dma_start(lin2_sb[:, :], lin2_w).then_inc(late_loaded, 16)
            sp.dma_start(lin_sb[:, :], lin_w).then_inc(late_loaded, 16)
            sp.dma_start(lin2_b_sb[:, :], lin2_b).then_inc(late_loaded, 16)
            sp.dma_start(lin_b_sb[:, :], lin_b.to_broadcast((TILE, FEAT))).then_inc(late_loaded, 16)

            sp.wait_ge(plan_ready, 1)
            passes = sp.value_load(passes_i[0:1, 0:1], min_val=1, max_val=MAX_PASSES)
            with sp.Fori(0, passes) as r:
                with sp.Fori(0, TURNS) as turn:
                    before = flat(r, turn)
                    for q in range(PAIRS_PER_TURN):
                        next_edges = sp.snap((turn * PAIRS_PER_TURN + q + 1) % PAIRS)
                        next_src = sp.snap((turn * PAIRS_PER_TURN + q + 2) % PAIRS)
                        if q == 0:
                            sp.wait_ge(l1_done, before * GROUPS_PER_TURN + 2)
                        load_edges(next_edges, 1 - q)
                        for b in range(2 * q, 2 * q + 2):
                            sp.wait_ge(gather_landed[b], (before + 1) * 16 * TILES_PER_GROUP)
                        load_src(next_src, q)

            for q in range(PAIRS_PER_TURN):
                sp.wait_ge(src_loaded[q], (passes * TURNS + 1) * 16)
            for half in range(2):
                c0, c1 = half * NODE_CHUNKS // 2, (half + 1) * NODE_CHUNKS // 2
                sp.wait_ge(normed_done, half + 1)
                sp.dma_start(out.rearrange("(c p) f -> p c f", p=TILE)[:, c0:c1, :], normed[:, c0:c1, :])\
                    .then_inc(out_stored, 16)
            sp.wait_ge(out_stored, 32)
        @block.gpsimd
        def _(pool):
            nc.gpsimd.iota(iota_i[:, :], pattern=[[1, MAX_PASSES * WINDOW]], base=0, channel_multiplier=0)\
                .then_inc(consts_ready, 1)
            nc.gpsimd.memset(ones[:, :], 1.0).then_inc(consts_ready, 1)
            nc.gpsimd.memset(ident[:, :], 0.0).then_inc(consts_ready, 1)
            pool.wait_ge(consts_ready, 3)
            nc.gpsimd.affine_select(out=ident[:, :], in_=ident[:, :], compare_op=ALU.not_equal, fill=1.0,
                                    base=0, pattern=[[-1, GROUPS]], channel_multiplier=1).then_inc(consts_ready, 1)
            pool.wait_ge(xf_stored, 16)
            pool.wait_ge(plan_ready, 1)
            passes = pool.value_load(passes_i[0:1, 0:1], min_val=1, max_val=MAX_PASSES)
            with pool.Fori(0, passes) as r:
                with pool.Fori(0, TURNS) as turn:
                    before = flat(r, turn)
                    for b in range(GROUPS_PER_TURN):
                        if b % 2 == 0:
                            pool.wait_ge(src_loaded[b // 2], (before + 1) * 16)
                        pool.wait_ge(message_done, before * GROUPS_PER_TURN + b + 1)
                        pool.sem_inc(group_begun, 1)
                        for t in range(TILES_PER_GROUP):
                            col = (b % 2) * TILES_PER_GROUP + t
                            nc.gpsimd.indirect_dma_start(
                                out=gathered[:, b, t, :], out_offset=None, in_=xf_dram[:, :],
                                in_offset=bass.IndirectOffsetOnAxis(ap=src_idx[:, b // 2, col:col + 1], axis=0),
                            ).then_inc(gather_landed[b], 16)

        @block.scalar
        def _(act):
            act.dma_start(w0_sb[0:EDGE_FEAT, :], f_w0).then_inc(w_loaded, 16)
            act.dma_start(w0_sb[ODD_BASE:ODD_BASE + EDGE_FEAT, :], f_w0).then_inc(w_loaded, 16)
            act.dma_start(b0_sb[:, :], f_b0).then_inc(w_loaded, 16)
            act.dma_start(w1_sb[:, :], f_w1).then_inc(w_loaded, 16)
            act.dma_start(b1_sb[:, :], f_b1).then_inc(w_loaded, 16)
            act.dma_start(w2_sb[:, :], f_w2).then_inc(w_loaded, 16)
            act.dma_start(b2_sb[:, :], f_b2).then_inc(w_loaded, 16)
            act.dma_start(w3_sb[:, :], f_w3).then_inc(w_loaded, 16)
            act.dma_start(b3_sb[:, :], f_b3.to_broadcast((TILE, FEAT))).then_inc(w_loaded, 16)
            act.wait_ge(clamped_ready, 2)
            nc.scalar.activation(cosine[:, :], clamped[:, :], ACT.Sin, bias=half_pi[:, 0:1],
                                 scale=-PI / CUTOFF).then_inc(cosine_ready, 1)
            for k, (c0, c1) in enumerate(chunk_cuts):
                act.wait_ge(xf_product, k + 1)
                nc.scalar.activation(xf_sb[:, c0:c1, :], xf_bank[k][0:TILE, 0:(c1 - c0) * FEAT]
                                     .rearrange("p (c f) -> p c f", f=FEAT), ACT.Copy).then_inc(xf_copied, 1)

            def gelu(out_ap, in_ap, bias, done):
                if bias is None:
                    nc.scalar.activation(out_ap, in_ap, GELU).then_inc(done, 1)
                else:
                    nc.scalar.activation(out_ap, in_ap, GELU, bias=bias[:, 0:1]).then_inc(done, 1)

            act.wait_ge(w_loaded, 9 * 16)
            for b in range(2):
                act.wait_ge(l1_done, b + 1)
                gelu(h1[:, b, :], ps1[b][:, 0:GROUP], b0_sb, act1_done)
            act.wait_ge(plan_ready, 1)
            passes = act.value_load(passes_i[0:1, 0:1], min_val=1, max_val=MAX_PASSES)
            with act.Fori(0, passes * TURNS) as before:
                for q in range(PAIRS_PER_TURN):
                    g = before * GROUPS_PER_TURN + 2 * q
                    for b in range(2):
                        act.wait_ge(l2_done, g + b + 1)
                        gelu(h2[:, b, :], ps23[b][:, 0:GROUP], b1_sb, act2_done)
                    for b in range(2):
                        act.wait_ge(l3_done, g + b + 1)
                        gelu(h3[:, b, :], ps23[b][:, 0:GROUP], b2_sb, act3_done)
                    for b in range(2):
                        act.wait_ge(l1_done, g + b + 3)
                        gelu(h1[:, b, :], ps1[b][:, 0:GROUP], b0_sb, act1_done)
                    for b in range(2):
                        act.wait_ge(bias4_done, g + b + 1)
                        gelu(h4[:, b, :, :], pre4[:, b, :, :], None, act4_done)

            act.wait_ge(late_loaded, 5 * 16)
            for k, (n0, n1) in enumerate(node_cuts):
                act.wait_ge(node2_done, k + 1)
                gelu(nodeT[:, n0:n1], node_bank[k][:, 0:n1 - n0], lin2_b_sb, node_gelu_done)
            for k, (c0, c1) in enumerate(chunk_cuts):
                act.wait_ge(var_done, k + 1)
                nc.scalar.activation(std[:, c0:c1].rearrange("p (c o) -> p c o", o=1), mean_var[:, c0:c1, 1:2],
                                     ACT.Sqrt, bias=eps[:, 0:1]).then_inc(std_done, 1)

        @block.tensor
        def _(pe):
            pe.wait_ge(x_loaded, 32)
            for k, (c0, c1) in enumerate(chunk_cuts):
                for c in range(c0, c1):
                    last = nc.tensor.matmul(xf_bank[k][0:TILE, (c - c0) * FEAT:(c - c0 + 1) * FEAT],
                                            xT_sb[:, c * TILE:(c + 1) * TILE], lin1_sb[:, :], start=True, stop=True)
                last.then_inc(xf_product, 1)
            pe.wait_ge(consts_ready, 4)
            pe.wait_ge(diag_ready, 2)
            nc.tensor.matmul(ps_agg[0][0:TILE, 0:2 * GROUPS], ones[:, :],
                             diag[:, :, :].rearrange("p a g -> p (a g)"), start=True, stop=True).then_inc(rows_ready, 1)

            def layer1(q):
                for b in range(2):
                    rows = slice(b * ODD_BASE, b * ODD_BASE + EDGE_FEAT)
                    nc.tensor.matmul(ps1[b][:, 0:GROUP], w0_sb[rows, :], edge_in[rows, q, :],
                                     start=True, stop=True).then_inc(l1_done, 1)

            def scatter(slot, bank_agg):
                for t in range(TILES_PER_GROUP):
                    last = nc.tensor.matmul(bank_agg[:, 0:WINDOW], message[:, slot, t, :], onehot[:, slot, t, :],
                                            start=(t == 0), stop=(t == TILES_PER_GROUP - 1))
                last.then_inc(scatter_done, 1)

            pe.wait_ge(w_loaded, 9 * 16)
            pe.wait_ge(edge_loaded[0], 32)
            layer1(0)
            pe.wait_ge(plan_ready, 1)
            passes = pe.value_load(passes_i[0:1, 0:1], min_val=1, max_val=MAX_PASSES)
            with pe.Fori(0, passes * TURNS) as before:
                for q in range(PAIRS_PER_TURN):
                    g = before * GROUPS_PER_TURN + 2 * q
                    for b in range(2):
                        pe.wait_ge(act1_done, g + b + 1)
                        nc.tensor.matmul(ps23[b][:, 0:GROUP], w1_sb[:, :], h1[:, b, :],
                                         start=True, stop=True).then_inc(l2_done, 1)
                    for b in range(2):
                        pe.wait_ge(message_done, g + b + 3)
                        pe.wait_ge(agg_added, g + b + 1)
                        scatter((2 * q + b - 2) % GROUPS_PER_TURN, ps_agg[b])
                        pe.wait_ge(act2_done, g + b + 1)
                        nc.tensor.matmul(ps23[b][:, 0:GROUP], w2_sb[:, :], h2[:, b, :],
                                         start=True, stop=True).then_inc(l3_done, 1)
                    if q == 0:
                        pe.wait_ge(edge_loaded[1], (before + 1) * 32)
                    else:
                        pe.wait_ge(edge_loaded[0], (before + 2) * 32)
                    layer1(1 - q)
                    for b in range(2):
                        pe.wait_ge(act3_done, g + b + 1)
                        for t in range(TILES_PER_GROUP):
                            last = nc.tensor.matmul(ps4[b][0:TILE, t * FEAT:(t + 1) * FEAT],
                                                    h3[:, b, t * TILE:(t + 1) * TILE], w3_sb[:, :],
                                                    start=True, stop=True)
                        last.then_inc(l4_done, 1)
            groups = passes * GROUPS
            for b in range(2):
                pe.wait_ge(message_done, groups + b + 3)
                pe.wait_ge(agg_added, groups + b + 1)
                scatter((b - 2) % GROUPS_PER_TURN, ps_agg[b])

            pe.wait_ge(late_loaded, 5 * 16)
            pe.wait_ge(agg_added, groups + 4)
            pe.wait_ge(act1_done, groups + 2)
            for k, (n0, n1) in enumerate(node_cuts):
                nc.tensor.matmul(node_bank[k][:, 0:n1 - n0], lin2_sb[:, :], aggT[:, n0:n1],
                                 start=True, stop=True).then_inc(node2_done, 1)
            for k, (c0, c1) in enumerate(chunk_cuts):
                pe.wait_ge(node_gelu_done, k + 1)
                for c in range(c0, c1):
                    last = nc.tensor.matmul(out_bank[k][0:TILE, (c - c0) * FEAT:(c - c0 + 1) * FEAT],
                                            nodeT[:, c * TILE:(c + 1) * TILE], lin_sb[:, :], start=True, stop=True)
                last.then_inc(node3_done, 1)

        @block.vector
        def _(dve):
            steps = [0]

            def chain(ins):
                steps[0] += 1
                ins.then_inc(setup_step, 1)
                dve.wait_ge(setup_step, steps[0])

            for b in (2, 3):
                nc.vector.memset(onehot[:, b, :, :], 0.0)
                nc.vector.memset(message[:, b, :, :], 0.0).then_inc(message_done, GROUPS_PER_TURN // 2)
            nc.vector.memset(aggT[:, :], 0.0)
            nc.vector.memset(half_pi[:, :], PI / 2).then_inc(clamped_ready, 1)
            nc.vector.memset(eps[:, :], LN_EPS)
            chain(nc.vector.memset(base_col[:, 0:2], 0))
            dve.wait_ge(tables_loaded, 48)
            nc.vector.tensor_scalar(clamped[:, :], dist[:, :], 0.0, CUTOFF, ALU.max, ALU.min).then_inc(clamped_ready, 1)
            chain(nc.vector.tensor_copy(dstg_f[:, :], dstg_i[:, :]))
            nc.vector.tensor_reduce(lo_hi[:, 0:1], dstg_f[:, :], axis=AX_X, op=ALU.min)
            chain(nc.vector.tensor_reduce(lo_hi[:, 1:2], dstg_f[:, :], axis=AX_X, op=ALU.max))
            chain(nc.vector.tensor_tensor(span[:, :], lo_hi[:, 1:2], lo_hi[:, 0:1], ALU.subtract))
            dve.wait_ge(consts_ready, 4)
            nc.vector.tensor_scalar(diag[:, 0, :], ident[:, :], lo_hi[:, 0:1], None, ALU.mult).then_inc(diag_ready, 1)
            nc.vector.tensor_scalar(diag[:, 1, :], ident[:, :], span[:, 0:1], None, ALU.mult).then_inc(diag_ready, 1)
            nc.vector.tensor_copy(iota_f[:, :], iota_i[:, :])
            nc.vector.tensor_copy(dst_f[:, :, :], dst_i[:, :, :])
            nc.vector.tensor_scalar(not_above[:, :], dist[:, :], CUTOFF, None, ALU.is_le)
            chain(nc.vector.tensor_scalar(inside[:, :], dist[:, :], 0.0, 0.5, ALU.is_ge, ALU.mult))
            dve.wait_ge(rows_ready, 1)
            starts = iota_f[0:1, :].rearrange("p (w n) -> p w n", n=WINDOW)[:, :, 0:1]
            chain(nc.vector.tensor_reduce(max_span[:, :], ps_agg[0][0:1, GROUPS:2 * GROUPS], axis=AX_X, op=ALU.max))
            chain(nc.vector.tensor_scalar(pass_needed[:, :], starts.rearrange("p w o -> p (w o)"), max_span[:, 0:1],
                                          None, ALU.is_le))
            chain(nc.vector.tensor_reduce(passes_f[:, :], pass_needed[:, :], axis=AX_X, op=ALU.add))
            nc.vector.tensor_copy(passes_i[:, :], passes_f[:, :])
            chain(nc.vector.tensor_tensor(
                base_raw[:, :, :], starts.to_broadcast((1, MAX_PASSES, GROUPS)),
                ps_agg[0][0:1, 0:GROUPS].rearrange("p (o g) -> p o g", o=1).to_broadcast((1, MAX_PASSES, GROUPS)),
                ALU.add))
            nc.vector.tensor_scalar(base_col[:, 2:], base_raw[:, :, :].rearrange("p w g -> p (w g)"), float(NODES),
                                    None, ALU.min).then_inc(plan_ready, 1)
            nc.vector.tensor_tensor(
                dst_rel[:, :, :], dst_f[:, :, :],
                ps_agg[0][0:TILE, 0:GROUPS].rearrange("p (g o) -> p g o", o=1)
                .to_broadcast((TILE, GROUPS, TILES_PER_GROUP)), ALU.subtract).then_inc(agg_added, 2)
            chain(nc.vector.tensor_tensor(inside[:, :], inside[:, :], not_above[:, :], ALU.mult))
            dve.wait_ge(cosine_ready, 1)
            chain(nc.vector.tensor_scalar(half_cos[:, :], cosine[:, :], 1.0, None, ALU.add))
            chain(nc.vector.tensor_tensor(cut[:, :, :].rearrange("p g t -> p (g t)"), half_cos[:, :], inside[:, :],
                                          ALU.mult))

            def add_window(entry, b):
                dve.wait_ge(scatter_done, entry + 1)
                dve.wait_ge(agg_added, entry + 2)
                col = dve.value_load(base_col[0:1, bass.ds(entry, 1)], min_val=0, max_val=NODES)
                window = aggT[:, bass.ds(col, WINDOW)]
                nc.vector.tensor_tensor(window, window, ps_agg[b][:, 0:WINDOW], ALU.add).then_inc(agg_added, 1)

            dve.wait_ge(plan_ready, 1)
            passes = dve.value_load(passes_i[0:1, 0:1], min_val=1, max_val=MAX_PASSES)
            with dve.Fori(0, passes) as r:
                with dve.Fori(0, TURNS) as turn:
                    before = flat(r, turn)
                    for q in range(PAIRS_PER_TURN):
                        g = before * GROUPS_PER_TURN + 2 * q
                        for b in range(2):
                            slot = 2 * q + b
                            here = turn * GROUPS_PER_TURN + slot
                            nodes = iota_f[:, bass.ds(r * WINDOW, WINDOW)].rearrange("p (o n) -> p o n", o=1)\
                                .to_broadcast((TILE, TILES_PER_GROUP, WINDOW))
                            dst = dst_rel[:, bass.ds(here, 1), :].rearrange("p o t -> p (o t)")\
                                .rearrange("p (t o) -> p t o", o=1).to_broadcast((TILE, TILES_PER_GROUP, WINDOW))
                            factor = cut[:, bass.ds(here, 1), :].rearrange("p o t -> p (o t)")\
                                .rearrange("p (t o) -> p t o", o=1).to_broadcast((TILE, TILES_PER_GROUP, WINDOW))
                            nc.vector.tensor_tensor(hit[:, slot, :, :], dst, nodes, ALU.is_equal).then_inc(hit_done, 1)
                            dve.wait_ge(hit_done, g + b + 1)
                            nc.vector.tensor_tensor(onehot[:, slot, :, :], hit[:, slot, :, :], factor, ALU.mult)
                        for b in range(2):
                            add_window(g + b, b)
                        for b in range(2):
                            dve.wait_ge(l4_done, g + b + 1)
                            nc.vector.tensor_tensor(
                                pre4[:, b, :, :], ps4[b][0:TILE, :].rearrange("p (t f) -> p t f", f=FEAT),
                                b3_sb[:, :].rearrange("p (o f) -> p o f", o=1)
                                .to_broadcast((TILE, TILES_PER_GROUP, FEAT)), ALU.add).then_inc(bias4_done, 1)
                        for b in range(2):
                            slot = 2 * q + b
                            dve.wait_ge(act4_done, g + b + 1)
                            dve.wait_ge(gather_landed[slot], (before + 1) * 16 * TILES_PER_GROUP)
                            nc.vector.tensor_tensor(message[:, slot, :, :], h4[:, b, :, :], gathered[:, slot, :, :],
                                                    ALU.mult).then_inc(message_done, 1)
            for b in range(2):
                add_window(passes * GROUPS + b, b)

            dve.wait_ge(late_loaded, 5 * 16)
            ln = [0]

            def ln_chain(ins):
                ln[0] += 1
                ins.then_inc(ln_step, 1)
                dve.wait_ge(ln_step, ln[0])

            ln_chain(nc.vector.tensor_tensor(x_plus_b[:, :, :], x_sb[:, :, :],
                                    lin_b_sb[:, :].rearrange("p (o f) -> p o f", o=1)
                                    .to_broadcast((TILE, NODE_CHUNKS, FEAT)), ALU.add))
            for k, (c0, c1) in enumerate(chunk_cuts):
                dve.wait_ge(node3_done, k + 1)
                ln_chain(nc.vector.tensor_tensor(
                    resid[:, c0:c1, :], x_plus_b[:, c0:c1, :],
                    out_bank[k][0:TILE, 0:(c1 - c0) * FEAT].rearrange("p (c f) -> p c f", f=FEAT), ALU.add))
                for c in range(c0, c1):
                    last = nc.vector.bn_stats(stats[:, c, :], resid[:, c, :])
                ln_chain(last)
                for c in range(c0, c1):
                    last = nc.vector.bn_aggr(mean_var[:, c, :], stats[:, c, :])
                last.then_inc(var_done, 1)
                dve.wait_ge(std_done, k + 1)
                ln_chain(nc.vector.reciprocal(rstd[:, c0:c1], std[:, c0:c1]))
                for c in range(c0, c1):
                    last = nc.vector.tensor_scalar(normed[:, c, :], resid[:, c, :], mean_var[:, c, 0:1],
                                                   rstd[:, c:c + 1], ALU.subtract, ALU.mult)
                    if c in (NODE_CHUNKS // 2 - 1, NODE_CHUNKS - 1):
                        last.then_inc(normed_done, 1)


_INS = ["xT", "x_nodes", "srcT", "dstT", "dst_groups", "weightT", "edge_attrT", "f_w0", "f_b0", "f_w1", "f_b1",
        "f_w2", "f_b2", "f_w3", "f_b3", "lin1_w", "lin2_w", "lin2_b", "lin_w", "lin_b"]


def kernel(**inputs):
    import numpy as np
    import concourse.bacc as bacc
    from concourse.bass_utils import run_bass_kernel_spmd

    get = {name: np.asarray(a) for name, a in inputs.items()}
    w = {name[len("L0_gnn_"):]: a for name, a in get.items() if name.startswith("L0_gnn_")}
    per_edge = lambda a: a.reshape(GROUPS * TILES_PER_GROUP, TILE).T
    data = {
        "xT": get["x"].T, "x_nodes": get["x"],
        "srcT": get["src"].reshape(PAIRS, 2 * TILES_PER_GROUP, TILE).transpose(0, 2, 1),
        "dstT": per_edge(get["dst"]), "dst_groups": get["dst"].reshape(GROUPS, GROUP),
        "weightT": per_edge(get["edge_weight"]),
        "edge_attrT": get["edge_attr_50"].reshape(PAIRS, 2, GROUP, EDGE_FEAT).transpose(0, 1, 3, 2),
    }
    for name in ("f_w0", "f_w1", "f_w2", "f_w3", "lin1_w", "lin2_w", "lin_w"):
        data[name] = w[name]
    for name in ("f_b0", "f_b1", "f_b2", "lin2_b"):
        data[name] = w[name].reshape(FEAT, 1)
    for name in ("f_b3", "lin_b"):
        data[name] = w[name].reshape(1, FEAT)

    nc = bacc.Bacc("TRN2", target_bir_lowering=False, num_devices=1)
    arrays, args = {}, []
    for name in _INS:
        a = np.ascontiguousarray(data[name])
        arrays[f"in_{name}"] = a
        args.append(nc.dram_tensor(f"in_{name}", a.shape, mybir.dt.from_np(a.dtype), kind="ExternalInput").ap())
    args.append(nc.dram_tensor("out_0", (NODES, FEAT), mybir.dt.float32, kind="ExternalOutput").ap())
    gnn_layer(nc, *args)
    result = run_bass_kernel_spmd(nc, [arrays], core_ids=[0])
    return result.results[0]["out_0"]
```
